# Optimizing a Trainium2 kernel written in Bass

```python
import numpy as np
import jax
import jax.numpy as jnp

def _softmax(x, axis=-1):
    return jax.nn.softmax(x, axis=axis)

def _gelu(x):
    return jax.nn.gelu(x, approximate=True)

def _silu(x):
    return jax.nn.silu(x)

def _sigmoid(x):
    return jax.nn.sigmoid(x)

def _layernorm(x, axis=-1, eps=1e-05):
    m = jnp.mean(x, axis=axis, keepdims=True)
    v = jnp.var(x, axis=axis, keepdims=True)
    return (x - m) / jnp.sqrt(v + eps)

def _scatter_add(tgt, idx, src, axis=0):
    return tgt.at[idx].add(src)

def _segment_sum(src, seg, n):
    return jax.ops.segment_sum(src, seg, n)
kernel_name = 'mk_xattn_ffn_d1_seqx_r8_8c8be4'

def setup_inputs(seed: int=0):
    np.random.seed(seed)
    _w = jnp.asarray

    def _rec_inputs():
        import jax
        import jax.numpy as jnp
        _rk = jax.random.key(seed)
        x = -0.000125 + 0.9999 * jax.random.normal(jax.random.fold_in(_rk, 1), (4, 256, 256), jnp.float32)
        _lenS = 256 - jax.random.randint(jax.random.fold_in(_rk, 7), (4,), 0, max(1, 256 // 4) + 1, jnp.int32)
        _lenS2 = 256 - jax.random.randint(jax.random.fold_in(_rk, 8), (4,), 0, max(1, 256 // 4) + 1, jnp.int32)
        _ctx_2048P = jax.random.normal(jax.random.fold_in(_rk, 11), (4, 16, 256), jnp.float32)
        _ctx_2048c = jax.random.dirichlet(jax.random.fold_in(_rk, 511), 0.3 * jnp.ones((16,), jnp.float32), (4, 256))
        _ctx_2048t = jnp.einsum('bsk,bkd->bsd', _ctx_2048c, _ctx_2048P)
        _ctx_2048t = _ctx_2048t * jax.lax.rsqrt(jnp.mean(jnp.square(_ctx_2048t)) + 1e-12) * 0.953939
        ctx_2048 = -0.00010331 + 0.999899 * (_ctx_2048t + 0.3 * jax.random.normal(jax.random.fold_in(_rk, 611), (4, 256, 256), jnp.float32))
        _validS = jnp.arange(256)[None, :] < _lenS[:, None]
        _validS2 = jnp.arange(256)[None, :] < _lenS2[:, None]
        _causal = jnp.tril(jnp.ones((256, 256), dtype=bool))
        mask_Bx1xS2_ff0 = jnp.where(jnp.ones((4, 1, 256), dtype=bool), 0.0, -1000000000.0).astype(jnp.float32)
        return (x, ctx_2048, mask_Bx1xS2_ff0)
    x, ctx_2048, mask_Bx1xS2_ff0 = _rec_inputs()

    def _L0_xattn_setup():
        import jax, jax.numpy as jnp
        import numpy as np
        FP8_E4M3_MAX = 448.0
        EPS = 1e-12

        def _fp8_quant_dequant(x):
            amax = jnp.max(jnp.abs(x))
            scale = FP8_E4M3_MAX / jnp.maximum(amax, EPS)
            q = jnp.clip(x * scale, -FP8_E4M3_MAX, FP8_E4M3_MAX).astype(jnp.float8_e4m3fn)
            return q.astype(jnp.float32) / scale
        key = jax.random.key(seed)
        k1, k2 = jax.random.split(key)
        B, M, K, N = (32, 64, 256, 256)
        inp = jax.random.normal(k1, (B, M, K), dtype=jnp.float32)
        weight = jax.random.normal(k2, (B, K, N), dtype=jnp.float32)
        bias = jnp.zeros((B, 1, N), dtype=jnp.float32)
        return {'input': inp, 'weight': weight, 'bias': bias}
    _L0_xattn_all = _L0_xattn_setup()
    _L0_xattn_in = {k: v for k, v in _L0_xattn_all.items() if k in ()}
    del _L0_xattn_all

    def _L0_ffn_setup():
        import jax, jax.numpy as jnp
        import numpy as np
        DIM = 256
        INTER = 176
        N_EXPERTS = 16
        TOP_K = 2
        N_SHARED = 2
        SHARED_INTER = N_SHARED * INTER

        def _swiglu(t, wa, wb, wo):
            h = jax.nn.silu(t @ wa.T) * (t @ wb.T)
            return h @ wo.T
        key = jax.random.key(seed)
        ks = jax.random.split(key, 9)
        s = 0.02
        return {'x': jax.random.normal(ks[0], (4, 256, DIM), dtype=jnp.float32), 'gate_w': jax.random.normal(ks[1], (N_EXPERTS, DIM), dtype=jnp.float32) * s, 'w1': jax.random.normal(ks[2], (N_EXPERTS, INTER, DIM), dtype=jnp.float32) * s, 'w2': jax.random.normal(ks[3], (N_EXPERTS, DIM, INTER), dtype=jnp.float32) * s, 'w3': jax.random.normal(ks[4], (N_EXPERTS, INTER, DIM), dtype=jnp.float32) * s, 'sw1': jax.random.normal(ks[5], (SHARED_INTER, DIM), dtype=jnp.float32) * s, 'sw2': jax.random.normal(ks[6], (DIM, SHARED_INTER), dtype=jnp.float32) * s, 'sw3': jax.random.normal(ks[7], (SHARED_INTER, DIM), dtype=jnp.float32) * s}
    _L0_ffn_all = _L0_ffn_setup()
    _L0_ffn_in = {k: v for k, v in _L0_ffn_all.items() if k in ('gate_w', 'w1', 'w2', 'w3', 'sw1', 'sw2', 'sw3')}
    del _L0_ffn_all
    return {'x': x, 'ctx_2048': ctx_2048, 'mask_Bx1xS2_ff0': mask_Bx1xS2_ff0, 'L0_ffn_gate_w': _L0_ffn_in['gate_w'], 'L0_ffn_w1': _L0_ffn_in['w1'], 'L0_ffn_w2': _L0_ffn_in['w2'], 'L0_ffn_w3': _L0_ffn_in['w3'], 'L0_ffn_sw1': _L0_ffn_in['sw1'], 'L0_ffn_sw2': _L0_ffn_in['sw2'], 'L0_ffn_sw3': _L0_ffn_in['sw3']}

def reference(x, ctx_2048, mask_Bx1xS2_ff0, L0_ffn_gate_w, L0_ffn_w1, L0_ffn_w2, L0_ffn_w3, L0_ffn_sw1, L0_ffn_sw2, L0_ffn_sw3):
    import jax
    import jax.numpy as jnp

    def _L0_xattn_ref(input, weight, bias):
        import jax, jax.numpy as jnp
        import numpy as np
        FP8_E4M3_MAX = 448.0
        EPS = 1e-12

        def _fp8_quant_dequant(x):
            amax = jnp.max(jnp.abs(x))
            scale = FP8_E4M3_MAX / jnp.maximum(amax, EPS)
            q = jnp.clip(x * scale, -FP8_E4M3_MAX, FP8_E4M3_MAX).astype(jnp.float8_e4m3fn)
            return q.astype(jnp.float32) / scale
        x_dq = _fp8_quant_dequant(input)
        w_dq = _fp8_quant_dequant(weight)
        out = jnp.einsum('bmk,bkn->bmn', x_dq, w_dq)
        out = out + bias
        return out

    def _L0_ffn_ref(x, gate_w, w1, w2, w3, sw1, sw2, sw3):
        import jax, jax.numpy as jnp
        import numpy as np
        DIM = 256
        INTER = 176
        N_EXPERTS = 16
        TOP_K = 2
        N_SHARED = 2
        SHARED_INTER = N_SHARED * INTER

        def _swiglu(t, wa, wb, wo):
            h = jax.nn.silu(t @ wa.T) * (t @ wb.T)
            return h @ wo.T
        shape = x.shape
        t = x.reshape(-1, DIM)
        scores = jax.nn.softmax(t @ gate_w.T, axis=-1)
        weights, indices = jax.lax.top_k(scores, TOP_K)
        y = jnp.zeros_like(t)
        for e in range(N_EXPERTS):
            w_e = jnp.sum(jnp.where(indices == e, weights, 0.0), axis=-1)
            y = y + _swiglu(t, w1[e], w3[e], w2[e]) * w_e[:, None]
        z = _swiglu(t, sw1, sw3, sw2)
        return (y + z).reshape(shape)
    x = x + _L0_xattn_ref(_layernorm(x, axis=-1), ctx_2048, mask_Bx1xS2_ff0)
    x = x + _L0_ffn_ref(_layernorm(x, axis=-1), L0_ffn_gate_w, L0_ffn_w1, L0_ffn_w2, L0_ffn_w3, L0_ffn_sw1, L0_ffn_sw2, L0_ffn_sw3)
    return x

_drawn_inputs = setup_inputs


def setup_inputs(seed=0):
    import zlib

    import numpy as np

    out = dict(_drawn_inputs(seed))
    spreads = {}
    factors = {'L0_ffn_gate_w': 8.0,
     'L0_ffn_w1': 8.0,
     'L0_ffn_w2': 8.0,
     'L0_ffn_w3': 8.0,
     'L0_ffn_sw1': 8.0,
     'L0_ffn_sw2': 8.0,
     'L0_ffn_sw3': 8.0}
    for name, (base, spread) in spreads.items():
        noise = np.random.default_rng([zlib.crc32(name.encode()), seed]).standard_normal(out[name].shape)
        drawn = base * np.exp(spread * noise) if base else spread * noise
        out[name] = jnp.asarray(drawn.astype(out[name].dtype))
    for name, factor in factors.items():
        out[name] = (out[name] * factor).astype(out[name].dtype)
    return out
```

```python
from contextlib import ExitStack

import concourse.bass as bass
from concourse import mybir

P = 128
B, S, D = 4, 256, 256
TOK = B * S
NT = TOK // P
E = 16
TOPK = 2
INTER = 176
NSH = 2
NW = NSH + E
DC = D // P
UP = 2 * INTER
REST = INTER - P
DUP = 64
WMAIN = DC * UP + D
WROW = WMAIN + D
HALF = WROW // 2
STACK_TMP = 4
MAXT = (TOPK * TOK - E) // P + E
NPAIR = TOPK * NT
FP8_MAX = 448.0
LN_EPS = 1e-5
PRE = 6
N0 = PRE * NSH
N1 = N0 + MAXT
NTILE = N1 + (NT - PRE) * NSH
XSLOT = 8
SCATTER_LAG = 10
YSLOT = 4
LO_GATING = (8, 10, 12, 14)
LO_STEPS = (30, 32, 34)
LO_ON_DVE = LO_GATING + LO_STEPS
LO_FIRST = 2
FUSED = 2
GATHER_AT = 34
HI_LN2 = 3
HI_STEP = 3
CTX_BUF = 4
EARLY = 4
UNROLL = 8


def build(nc, x_in, ctx_in, mask_in, gate_in, w_in, out):
    F32, F32R, BF16 = mybir.dt.float32, mybir.dt.float32r, mybir.dt.bfloat16
    F16, I32 = mybir.dt.float16, mybir.dt.int32
    ALU, ACT, AX = mybir.AluOpType, mybir.ActivationFunctionType, mybir.AxisListType

    x_rows = x_in.rearrange("b (p h) d -> b p (h d)", p=P)
    out_rows = out.rearrange("b (p h) d -> b p (h d)", p=P)
    ctx_rows = ctx_in.rearrange("b (c p) d -> p b c d", p=P)

    es = ExitStack()
    with es:
        def sb(name, shape, dt=F32):
            return es.enter_context(nc.sbuf_tensor(name, shape, dt))

        def sem(name):
            return es.enter_context(nc.semaphore(name))

        t_dram = nc.dram_tensor("t_rows", (TOK, D), F32, kind="Internal").ap()
        y_dram = nc.dram_tensor("y_pairs", (TOPK * TOK, D), F32, kind="Internal").ap()
        y_rows = y_dram.rearrange("(k b p h) d -> k b p (h d)", k=TOPK, b=B, p=P)
        t_rows = t_dram.rearrange("(b p h) d -> b p (h d)", b=B, p=P)

        with nc.sbuf_tensor("hi_raw", [P, NW * WROW], F32) as hi_raw:
            with nc.sbuf_tensor("lo_raw", [P, NW * WMAIN], F32) as lo_raw:
                pass
        w_hi = sb("w_hi", [P, NW * WROW], F32R)
        w_lo = sb("w_lo", [P, NW * WMAIN], F32R)
        stack_hi = sb("stack_hi", [P, STACK_TMP, D], F32R)
        x1 = sb("x1", [P, NT, D])
        r1 = sb("r1", [P, NT, D])
        r2 = sb("r2", [P, NT * D])
        mx_buf = sb("mx_buf", [P, YSLOT * D])
        mc_buf = sb("mc_buf", [P, CTX_BUF, D])
        q_ctx = sb("q_ctx", [P, NT, D], BF16)
        q_xT = sb("q_xT", [P, 2, 2 * D], BF16)
        xT_hi = sb("xT_hi", [P, 2, D], F32R)
        xT_lo = sb("xT_lo", [P, 2, D], F32R)
        hT_hi = sb("hT_hi", [P, 2, D], F32R)
        hT_lo = sb("hT_lo", [P, 2, D], F32R)
        gate = sb("gate", [P, DC * E])
        gate_hl = sb("gate_hl", [P, DC, 2 * E], F32R)
        ident = sb("ident", [P, P])
        ones_row = sb("ones_row", [1, P])
        lower = sb("lower", [P, P], BF16)
        ones_bf = sb("ones_bf", [P, P], BF16)
        chosen = sb("chosen", [P, NT + 1, E], BF16)
        small = sb("small", [P, 128])
        smalli = sb("smalli", [P, 96], I32)
        ex_row = sb("ex_row", [1, 32], I32)

        y_norm = r2[:, :]
        vT = r2[:, :]
        mterm = mx_buf[:, :].rearrange("p (k n) -> p k n", k=2)
        xg = [r2[:, k * D:(k + 1) * D] for k in range(4)] + [r1[:, i, :] for i in (NT - 2, NT - 1, 0, 1)]
        sil = r2[:, 1024:1024 + 2 * INTER].rearrange("p (k f) -> p k f", k=2)
        hbuf = r2[:, 1408:1408 + 2 * D].rearrange("p (k f) -> p k f", k=2)
        yo = mx_buf[:, :].rearrange("p (k d) -> p k d", k=YSLOT)
        y_buf = lo_raw[:, NSH * WMAIN:NSH * WMAIN + TOPK * NT * D].rearrange("p (k b d) -> p k b d", k=TOPK, b=B)
        qf = q_ctx[:, :, :].rearrange("p a d -> p (a d)").bitcast(F32)
        rt = [qf[:, 128 * k:128 * (k + 1)].rearrange("p (i e) -> p i e", e=E) for k in range(8)]
        probs, ta, tb, e1, e2, slots = rt[0:6]
        rt2 = qf[:, 768:1024]
        onehot_p = mx_buf[:, :].bitcast(F16).rearrange("p (q s) -> p q s", s=P)
        onehot_t = q_xT[:, :, :].rearrange("p a d -> p (a d)").bitcast(F16)[:, 0:NPAIR * 32] \
            .rearrange("p (q j) -> p q j", j=32)
        mv = small[:, 0:2 * NT].rearrange("p (i s) -> p i s", s=2)
        rstd = small[:, 16:16 + NT]
        dev = small[:, 24:24 + NT]
        shift = small[:, 104:104 + NT]
        warm = small[:, 124:127]
        var_eps, neghalf = small[:, 32:32 + NT], small[:, 96:96 + NT]
        eps = small[:, 121:122]
        am_x, am_c = small[:, 40:44], small[:, 44:45]
        sc_x, sc_c, dequant = small[:, 45:46], small[:, 46:47], small[:, 47:48]
        am_x1 = small[:, 48:49]
        gx, gc = small[0:1, 49:50], small[0:1, 50:51]
        dq_x, dq_c = small[:, 51:52], small[:, 52:53]
        rec_x, rec_c = small[:, 53:54], small[:, 54:55]
        red = small[:, 56:64]
        sc_x20, sc_c20 = small[:, 122:123], small[:, 123:124]
        upper = small[:, 55:56]
        posf = small[:, 64:64 + NPAIR]
        stats = sb("stats", [P, NT, 6])
        red2 = sb("red2", [P, NT])
        top = sb("top", [P, NT, 8])
        top_e = sb("top_e", [P, NT, 8], mybir.dt.uint32)
        nt_t = sb("nt_t", [P, 3 * E])
        pos_i = smalli[:, 0:NPAIR]
        pos_p = smalli[:, NPAIR:2 * NPAIR]
        pos_j = smalli[:, 2 * NPAIR:3 * NPAIR]
        token_of = smalli[:, 48:48 + 32]
        spent = mc_buf[:, :, :].rearrange("p a d -> p (a d)").bitcast(F16)
        iota_p, iota_j = spent[:, 0:P], spent[:, P:P + 32]
        before = spent[:, 256:256 + E * E].rearrange("p (a b) -> p a b", b=E)
        spent32 = spent.bitcast(F32)[:, 256:512]
        thr = spent32[:, 0:NT]
        tok_id = spent32[:, 32:32 + NPAIR]
        dest_of = spent32[:, 64:96].bitcast(I32)

        bank = [es.enter_context(nc.psum_tensor(f"bank{k}", [P, 512], F32)) for k in range(8)]
        xT_ps = [bank[0], bank[1]]
        up_ps = [bank[2], bank[3]]
        hT_ps = bank[4]
        route_ps = bank[5]
        y_ps = [bank[6], bank[7]]
        att_ps = [bank[4], bank[5], bank[6], bank[7]]

        x_loaded = [sem(f"x_loaded{b}") for b in range(B)]
        ctx_loaded, gate_loaded = sem("ctx_loaded"), sem("gate_loaded")
        w_loaded = [sem(f"w_loaded{e}") for e in range(NW)]
        consts_made = sem("consts_made")
        var_ready, rstd_ready = sem("var_ready"), sem("rstd_ready")
        dev_ready, norm_ready = sem("dev_ready"), sem("norm_ready")
        y_made = sem("y_made")
        yT_done, mask_added = sem("yT_done"), [sem(f"mask_added{b}") for b in range(B)]
        amax_part, amax_row, amax_one, amax_all = sem("amax_part"), sem("amax_row"), sem("amax_one"), sem("amax_all")
        ctx_scale_made, x_scale_made = sem("ctx_scale_made"), sem("x_scale_made")
        ctx_scaled, ctx_term = sem("ctx_scaled"), sem("ctx_term")
        ctx_quant = sem("ctx_quant")
        x_scaled, x_quant, att_done = sem("x_scaled"), sem("x_quant"), sem("att_done")
        t_made, t_stored = sem("t_made"), [sem(f"t_stored{b}") for b in range(B)]
        w_hi_made, w_lo_made, w_lo_made_v = sem("w_hi_made"), sem("w_lo_made"), sem("w_lo_made_v")
        gate_hi_made, gate_split, gate_done = sem("gate_hi_made"), sem("gate_split"), sem("gate_done")
        shifted, exp_made = sem("shifted"), sem("exp_made")
        chosen_made, prefix_done = sem("chosen_made"), sem("prefix_done")
        onehot_made, table_done, table_made, experts_made = (
            sem("onehot_made"), sem("table_done"), sem("table_made"), sem("experts_made"))
        xT_in_psum, xT_hi_made, xT_split = sem("xT_in_psum"), sem("xT_hi_made"), sem("xT_split")
        up_done, silu_made, h_made = sem("up_done"), sem("silu_made"), sem("h_made")
        hT_in_psum, hT_hi_made, hT_split = sem("hT_in_psum"), sem("hT_hi_made"), sem("hT_split")
        y_done, y_copied, z_added = sem("y_done"), sem("y_copied"), sem("z_added")
        x_gathered = [sem(f"x_gathered{k}") for k in range(XSLOT)]
        y_scattered = [sem(f"y_scattered{k}") for k in range(YSLOT)]
        y_loaded = [[sem(f"y_loaded{k}_{b}") for b in range(B)] for k in range(TOPK)]
        mixed, out_stored = sem("mixed"), sem("out_stored")
        dve_link, pool_link, act_link = sem("dve_link"), sem("pool_link"), sem("act_link")

        block = es.enter_context(nc.Block())

        def static(n):
            return isinstance(n, int)

        def routed(n):
            return (not static(n)) or N0 <= n < N1

        def order(n):
            return n // NSH if n < N0 else PRE + (n - N1) // NSH

        def token_tile(n):
            return (order(n) - FUSED) % NT

        def index(n):
            if routed(n):
                return n - N0 + PRE
            return n // NSH if n < N0 else PRE + MAXT + (n - N1) // NSH

        def opens(n):
            return routed(n) or n % NSH == (0 if n < N0 else N1 % NSH)

        def turned(n):
            return index(n) + NT - FUSED

        def turns(n):
            return opens(n) and (routed(n) or index(n) >= FUSED)

        def closes(n):
            return routed(n) or n + 1 >= NTILE or index(n + 1) != index(n)

        def last_user(i):
            return max(n for n in range(NTILE) if index(n) == i)

        def emptied_wait(eng, n):
            if not static(n):
                eng.wait_ge(y_copied, n - N0 - 1)
            elif index(n) >= 2:
                m = last_user(index(n) - 2)
                if routed(m):
                    eng.wait_ge(y_copied, m - N0 + 1)
                else:
                    eng.wait_ge(z_added, order(m) + 1)

        def main_cols(k):
            e, half = k // 2, k % 2
            lo0 = e * WMAIN + half * HALF
            return slice(lo0, lo0 + (WMAIN - HALF if half else HALF)), e * WROW + half * HALF

        def stack_cols(k):
            return slice(k // 2 * WROW + WMAIN, (k // 2 + 1) * WROW)

        def lo_before(k):
            return sum(m not in LO_ON_DVE for m in range(k))

        def split_lo(eng, k):
            eng.wait_ge(w_hi_made, k + 1)
            lo, hi0 = main_cols(k)
            hi = slice(hi0, hi0 + lo.stop - lo.start)
            last = eng.tensor_tensor(w_lo[:, lo], lo_raw[:, lo], w_hi[:, hi].bitcast(F32), ALU.subtract)
            if k % 2 == 1:
                st = stack_cols(k)
                last = eng.tensor_tensor(w_hi[:, st], hi_raw[:, st],
                                         stack_hi[:, k // 2 % STACK_TMP, :].bitcast(F32), ALU.subtract)
            last.then_inc(w_lo_made_v if k in LO_ON_DVE else w_lo_made, 1)

        LOOP0 = N0 + 1 + YSLOT
        LOOP1 = N1 - 2
        assert (LOOP1 - LOOP0) % UNROLL == 0 and UNROLL % XSLOT == 0 and UNROLL % YSLOT == 0

        def exists(n):
            return (not static(n)) or 0 <= n < NTILE

        def run_steps(eng, first, last, step, body_start=None):
            s = first
            while s < last:
                if s == LOOP0:
                    with eng.Fori(0, (LOOP1 - LOOP0) // UNROLL) as it:
                        if body_start:
                            body_start(it * UNROLL + LOOP0)
                        for k in range(UNROLL):
                            step(it * UNROLL + (LOOP0 + k), LOOP0 + k)
                    s = LOOP1
                else:
                    step(s, s)
                    s += 1

        def scattered_before(s, sk):
            j, jk = s - 1 - N0, sk - 1 - N0
            if static(s):
                return 16 * (j // YSLOT)
            return (s - sk) * (16 // YSLOT) + 16 * (jk // YSLOT)

        @block.sync
        def _(sp):
            for b in range(B):
                sp.dma_start(x1[:, 2 * b:2 * b + 2, :].rearrange("p h d -> p (h d)"),
                             x_rows[b]).then_inc(x_loaded[b], 16)
                if b == 1:
                    sp.dma_start(r1[:, :, :].rearrange("p (b c) d -> p b c d", b=B), ctx_rows) \
                        .then_inc(ctx_loaded, 16)
            sp.dma_start(gate[:, :], gate_in).then_inc(gate_loaded, 16)
            for e in range(NW):
                if e == EARLY:
                    for b in range(B):
                        sp.wait_ge(mask_added[b], 16)
                sp.dma_start(lo_raw[:, e * WMAIN:(e + 1) * WMAIN], w_in[e, :, 0:WMAIN]) \
                    .then_inc(w_loaded[e], 16)
                sp.dma_start(hi_raw[:, stack_cols(2 * e)], w_in[e, :, WMAIN:WROW]) \
                    .then_inc(w_loaded[e], 16)
            for b in range(B):
                sp.wait_ge(t_made, 2 * b + 2)
                sp.dma_start(t_rows[b], r1[:, 2 * b:2 * b + 2, :].rearrange("p h d -> p (h d)")) \
                    .then_inc(t_stored[b], 16)

            for k in range(YSLOT):
                sp.wait_ge(y_scattered[k], 16 * len(range(k, MAXT, YSLOT)))
            for b in range(B):
                for k in range(TOPK):
                    sp.dma_start(y_buf[:, k, b, :], y_rows[k, b]).then_inc(y_loaded[k][b], 16)
            for b in range(B - 1):
                sp.wait_ge(mixed, 2 * b + 2)
                sp.dma_start(out_rows[b], x1[:, 2 * b:2 * b + 2, :].rearrange("p h d -> p (h d)")) \
                    .then_inc(out_stored, 16)
            for h in range(2):
                sp.wait_ge(mixed, NT - 1 + h)
                sp.dma_start(out_rows[B - 1][:, h * D:(h + 1) * D], x1[:, NT - 2 + h, :]).then_inc(out_stored, 16)
            sp.wait_ge(out_stored, 16 * (B + 1))

        @block.gpsimd
        def _(pool):
            links = [0]

            def link(ins):
                links[0] += 1
                ins.then_inc(pool_link, 1)
                pool.wait_ge(pool_link, links[0])

            nc.gpsimd.memset(eps, LN_EPS)
            nc.gpsimd.memset(ident[:, :], 0.0)
            nc.gpsimd.memset(ones_row[:, :], 1.0)
            nc.gpsimd.memset(ones_bf[:, :], 1.0)
            nc.gpsimd.memset(lower[:, :], 0.0)
            nc.gpsimd.memset(upper, 1.0)
            nc.gpsimd.memset(neghalf, -0.5)
            link(nc.gpsimd.memset(chosen[:, NT, :], 0.0))
            nc.gpsimd.affine_select(out=upper, in_=upper, compare_op=ALU.is_ge, fill=0.0,
                                    base=-DUP, pattern=[[0, 1]], channel_multiplier=1)
            nc.gpsimd.affine_select(out=ident[:, :], in_=ident[:, :], compare_op=ALU.not_equal, fill=1.0,
                                    base=0, pattern=[[-1, P]], channel_multiplier=1)
            nc.gpsimd.affine_select(out=lower[:, :], in_=lower[:, :], compare_op=ALU.is_ge, fill=1.0,
                                    base=0, pattern=[[-1, P]], channel_multiplier=1).then_inc(consts_made, 1)
            for b in range(B):
                c = slice(2 * b, 2 * b + 2)
                pool.wait_ge(var_ready, b + 1)
                nc.gpsimd.tensor_tensor(rstd[:, c], var_eps[:, c], neghalf[:, c], ALU.pow).then_inc(rstd_ready, 1)
                if b >= B - LO_FIRST:
                    split_lo(nc.gpsimd, b - (B - LO_FIRST))

            def add_mask(b):
                pool.wait_ge(y_made, 2 * b + 2)
                pool.dma_start(x1[:, 2 * b:2 * b + 2, :], mask_in[b:b + 1].broadcast_to([P, 2, D]), accum_op=ALU.add) \
                    .then_inc(mask_added[b], 16)

            def ctx_round(c):
                pool.wait_ge(ctx_term, c + 1)
                link(nc.gpsimd.tensor_tensor(r1[:, c, :], r1[:, c, :], mc_buf[:, c % CTX_BUF, :], ALU.add))
                nc.gpsimd.tensor_tensor(q_ctx[:, c, :], mc_buf[:, c % CTX_BUF, :], r1[:, c, :], ALU.subtract) \
                    .then_inc(ctx_quant, 1)

            for c in range(NT):
                if 1 <= c <= B:
                    add_mask(c - 1)
                ctx_round(c)
            pool.wait_ge(ctx_quant, NT)
            nc.gpsimd.iota(iota_p, pattern=[[1, P]], base=0, channel_multiplier=0, allow_small_or_imprecise_dtypes=True)
            nc.gpsimd.iota(iota_j, pattern=[[1, 32]], base=0, channel_multiplier=0, allow_small_or_imprecise_dtypes=True)
            nc.gpsimd.iota(thr, pattern=[[P, NT]], base=0, channel_multiplier=0, allow_small_or_imprecise_dtypes=True)
            nc.gpsimd.iota(tok_id, pattern=[[TOK, TOPK], [S, B], [1, 2]], base=1, channel_multiplier=2,
                           allow_small_or_imprecise_dtypes=True)
            link(nc.gpsimd.memset(before, 0.0))
            nc.gpsimd.affine_select(out=before, in_=before, compare_op=ALU.is_ge, fill=1.0,
                                    base=0, pattern=[[-1, E], [1, E]], channel_multiplier=0).then_inc(consts_made, 1)

            def gather(j):
                if XSLOT // 2 <= j < XSLOT:
                    pool.wait_ge(xT_in_psum, NT + 2)
                if j >= XSLOT:
                    pool.wait_ge(xT_in_psum, NT - FUSED + PRE + j - XSLOT + 1)
                pool.indirect_dma_start(xg[j % XSLOT], None, t_dram,
                                        bass.IndirectOffsetOnAxis(ap=token_of[:, j:j + 1], axis=0)) \
                    .then_inc(x_gathered[j % XSLOT], 16)

            def scatter(j):
                pool.wait_ge(y_copied, j + 1)
                pool.indirect_dma_start(y_dram, bass.IndirectOffsetOnAxis(ap=dest_of[:, j:j + 1], axis=0),
                                        yo[:, j % YSLOT, :], None, bounds_check=TOPK * TOK - 1, oob_is_err=False) \
                    .then_inc(y_scattered[j % YSLOT], 16)

            for k in range(LO_FIRST, 2 * NW):
                if k == GATHER_AT:
                    for b in range(B):
                        pool.wait_ge(t_stored[b], 16)
                    pool.wait_ge(table_made, 1)
                    for j in range(XSLOT // 2):
                        gather(j)
                if k not in LO_ON_DVE:
                    split_lo(nc.gpsimd, k)
            for j in range(XSLOT // 2, MAXT + SCATTER_LAG):
                if j < MAXT:
                    gather(j)
                if 0 <= j - SCATTER_LAG < MAXT:
                    scatter(j - SCATTER_LAG)

        @block.scalar
        def _(act):
            def split_hi(k):
                act.wait_ge(w_loaded[k // 2], 32)
                lo, hi0 = main_cols(k)
                last = nc.scalar.activation(w_hi[:, hi0:hi0 + lo.stop - lo.start], lo_raw[:, lo], ACT.Copy)
                if k % 2 == 1:
                    if k >= 2 * STACK_TMP:
                        act.wait_ge(w_lo_made, lo_before(k - 2 * STACK_TMP + 1))
                    last = nc.scalar.activation(stack_hi[:, k // 2 % STACK_TMP, :],
                                                hi_raw[:, stack_cols(k)], ACT.Copy, scale=upper)
                last.then_inc(w_hi_made, 1)

            hi = iter(range(2 * NW))

            def split_some(n):
                for _ in range(n):
                    k = next(hi, None)
                    if k is not None:
                        split_hi(k)

            def deviation(b):
                c = slice(2 * b, 2 * b + 2)
                act.wait_ge(var_ready, B + b + 1)
                nc.scalar.activation(dev[:, c], mv[:, c, 1], ACT.Sqrt, bias=eps).then_inc(dev_ready, 1)

            def scale_x(b):
                if b >= 2:
                    act.wait_ge(x_quant, b - 1)
                nc.scalar.activation(vT[:, 512 * b:512 * (b + 1)], bank[b][:, :], ACT.Copy, scale=sc_x)
                nc.scalar.activation(mterm[:, b % 2, :], bank[b][:, :], ACT.Copy, scale=sc_x20).then_inc(x_scaled, 1)

            def scale_ctx(c):
                if c >= CTX_BUF:
                    act.wait_ge(ctx_quant, c - CTX_BUF + 1)
                nc.scalar.activation(mc_buf[:, c % CTX_BUF, :], r1[:, c, :], ACT.Copy, scale=sc_c20) \
                    .then_inc(act_link, 1)
                act.wait_ge(act_link, c + 1)
                nc.scalar.activation(r1[:, c, :], r1[:, c, :], ACT.Copy, scale=sc_c).then_inc(ctx_scaled, 1)

            act.wait_ge(consts_made, 1)
            nc.scalar.activation(warm[:, 0:1], eps, ACT.Sqrt)
            act.wait_ge(gate_loaded, 16)
            nc.scalar.activation(gate_hl[:, :, 0:E], gate[:, :].rearrange("p (c e) -> p c e", c=DC), ACT.Copy) \
                .then_inc(gate_hi_made, 1)
            split_some(LO_FIRST)
            act.wait_ge(ctx_scale_made, 1)
            for c in range(5):
                scale_ctx(c)
            split_some(1)
            scale_ctx(5)
            act.wait_ge(x_scale_made, 1)
            act.wait_ge(yT_done, NT)
            scale_x(0)
            scale_ctx(6)
            scale_x(1)
            scale_ctx(7)
            split_some(1)
            scale_x(2)
            split_some(1)
            scale_x(3)

            def x_high(u, uk, n):
                act.wait_ge(xT_in_psum, u + 1)
                if not static(u):
                    act.wait_ge(up_done, n - 1)
                elif u >= NT:
                    act.wait_ge(up_done, last_user(u - NT) + 1)
                elif u >= 2:
                    act.wait_ge(gate_done, u - 1)
                nc.scalar.activation(xT_hi[:, uk % 2, :], xT_ps[uk % 2][:, 0:D], ACT.Copy).then_inc(xT_hi_made, 1)

            def normalise(b):
                act.wait_ge(norm_ready, b + 1)
                for i in (2 * b, 2 * b + 1):
                    nc.scalar.activation(r1[:, i, :], x1[:, i, :], ACT.Identity, scale=rstd[:, i:i + 1],
                                         bias=shift[:, i:i + 1]).then_inc(t_made, 1)

            def x_highs(b):
                for i in (2 * b, 2 * b + 1):
                    x_high(i, i, None)

            deviation(0)
            normalise(0)
            x_highs(0)
            split_some(1)
            deviation(1)
            normalise(1)
            split_some(2)
            x_highs(1)
            split_some(2)
            deviation(2)
            normalise(2)
            x_high(4, 4, None)
            deviation(3)
            x_high(5, 5, None)
            normalise(3)
            split_some(HI_LN2)
            x_highs(3)
            split_some(HI_LN2)
            nc.scalar.activation(warm[:, 1:2], eps, ACT.Exp)

            def step(s, sk):
                if exists(s + 2) and turns(s + 2):
                    x_high(turned(s + 2), turned(sk + 2), s + 2)
                if exists(s + 1):
                    act.wait_ge(up_done, s + 2)
                    if not static(s) or s >= 1:
                        act.wait_ge(h_made, s)
                    nc.scalar.activation(sil[:, (sk + 1) % 2, :], up_ps[(sk + 1) % 2][:, 0:INTER], ACT.Silu) \
                        .then_inc(silu_made, 1)
                if exists(s):
                    act.wait_ge(hT_in_psum, s + 1)
                    if not static(s) or s >= 2:
                        act.wait_ge(y_done, s - 1)
                    nc.scalar.activation(hT_hi[:, sk % 2, :], hT_ps[:, 0:D], ACT.Copy).then_inc(hT_hi_made, 1)
                if exists(s - 1) and routed(s - 1):
                    j, jk = s - 1 - N0, sk - 1 - N0
                    act.wait_ge(y_done, s)
                    if not static(s) or j >= YSLOT:
                        act.wait_ge(y_scattered[jk % YSLOT], scattered_before(s, sk))
                    nc.scalar.activation(yo[:, jk % YSLOT, :], y_ps[index(sk - 1) % 2][:, 0:D], ACT.Copy) \
                        .then_inc(y_copied, 1)
                if static(s) and s < N0:
                    split_some(HI_STEP)

            step(-2, -2)
            act.wait_ge(shifted, 1)
            nc.scalar.activation(ta, tb, ACT.Exp).then_inc(exp_made, 1)
            nc.scalar.activation(warm[:, 2:3], eps, ACT.Silu)
            run_steps(act, -1, NTILE + 1, step)

        @block.vector
        def _(dve):
            links = [0]

            def link(ins):
                links[0] += 1
                ins.then_inc(dve_link, 1)
                dve.wait_ge(dve_link, links[0])

            v = nc.vector

            def moments(b):
                tiles = (2 * (b % B), 2 * (b % B) + 1)
                for i in tiles:
                    last = v.bn_stats(stats[:, i, :], x1[:, i, :])
                link(last)
                for i in tiles:
                    last = v.bn_aggr(mv[:, i, :], stats[:, i, :])
                if b < B:
                    link(last)
                    c = slice(tiles[0], tiles[1] + 1)
                    last = v.tensor_scalar(var_eps[:, c], mv[:, c, 1], LN_EPS, None, ALU.add)
                last.then_inc(var_ready, 1)

            def norm_y(b):
                dve.wait_ge(rstd_ready, b + 1)
                for i in (2 * b, 2 * b + 1):
                    v.tensor_scalar(y_norm[:, i * D:(i + 1) * D], x1[:, i, :], mv[:, i, 0:1], rstd[:, i:i + 1],
                                    ALU.subtract, ALU.mult).then_inc(y_made, 1)

            def inverse(b):
                c = slice(2 * b, 2 * b + 2)
                dve.wait_ge(dev_ready, b + 1)
                link(v.reciprocal(rstd[:, c], dev[:, c]))
                v.scalar_tensor_tensor(shift[:, c], mv[:, c, 0], -1.0, rstd[:, c], ALU.mult, ALU.mult) \
                    .then_inc(norm_ready, 1)

            def magnitude(b):
                dve.wait_ge(y_made, 2 * b + 2)
                return v.tensor_reduce(am_x[:, b:b + 1], y_norm[:, 512 * b:512 * (b + 1)], AX.X, ALU.max,
                                       apply_absolute_value=True)

            def largest(one, n):
                dve.wait_ge(amax_row, n)
                v.tensor_reduce(one, att_ps[3 - n][0:1, 0:P], AX.X, ALU.max).then_inc(amax_one, 1)

            def scales(part, rec, scale, scale20, dq, n, done):
                dve.wait_ge(amax_all, n)
                link(v.tensor_scalar(part, att_ps[3 - n][:, P:P + 1], 1e-12, None, ALU.max))
                link(v.reciprocal(rec, part))
                v.tensor_scalar(dq, part, 1.0 / FP8_MAX, None, ALU.mult)
                v.tensor_scalar(scale20, rec, FP8_MAX, 2.0 ** 20, ALU.mult, ALU.mult)
                v.tensor_scalar(scale, rec, FP8_MAX, None, ALU.mult).then_inc(done, 1)

            def leading(term):
                return v.tensor_scalar(term.bitcast(I32), term.bitcast(I32), 0x7F800000, 0x00400000,
                                       ALU.bitwise_and, ALU.bitwise_or)

            floor = 1.5 * 2.0 ** (20 - 6)

            def round_fp8(q, val, term):
                link(leading(term))
                link(v.scalar_tensor_tensor(val, term, floor, val, ALU.max, ALU.add))
                return v.scalar_tensor_tensor(q, term, floor, val, ALU.max, ALU.subtract)

            def ctx_terms(c):
                dve.wait_ge(ctx_scaled, c + 1)
                term = mc_buf[:, c % CTX_BUF, :]
                link(leading(term))
                v.tensor_scalar(term, term, floor, None, ALU.max).then_inc(ctx_term, 1)

            def quantise_x(b):
                dve.wait_ge(x_scaled, b + 1)
                if b >= 2:
                    dve.wait_ge(att_done, b - 1)
                round_fp8(q_xT[:, b % 2, :], vT[:, 512 * b:512 * (b + 1)], mterm[:, b % 2, :]).then_inc(x_quant, 1)

            def attend(b):
                dve.wait_ge(mask_added[b], 16)
                dve.wait_ge(att_done, b + 1)
                xb = x1[:, 2 * b:2 * b + 2, :].rearrange("p h d -> p (h d)")
                link(v.scalar_tensor_tensor(xb, att_ps[b][:, :], dequant, xb, ALU.mult, ALU.add))
                moments(B + b)

            def x_low(u, uk):
                dve.wait_ge(xT_hi_made, u + 1)
                v.tensor_tensor(xT_lo[:, uk % 2, :], xT_ps[uk % 2][:, 0:D], xT_hi[:, uk % 2, :].bitcast(F32),
                                ALU.subtract).then_inc(xT_split, 1)

            dve.wait_ge(x_loaded[0], 16)
            moments(0)
            dve.wait_ge(x_loaded[1], 16)
            moments(1)
            dve.wait_ge(ctx_loaded, 16)
            v.tensor_reduce(am_c, r1[:, :, :].rearrange("p a d -> p (a d)"), AX.X, ALU.max,
                            apply_absolute_value=True).then_inc(amax_part, 1)
            norm_y(0)
            dve.wait_ge(x_loaded[2], 16)
            moments(2)
            largest(gc, 1)
            scales(am_c, rec_c, sc_c, sc_c20, dq_c, 1, ctx_scale_made)
            norm_y(1)
            dve.wait_ge(x_loaded[3], 16)
            moments(3)
            magnitude(0)
            norm_y(2)
            ctx_terms(0)
            magnitude(1)
            norm_y(3)
            ctx_terms(1)
            magnitude(2)
            link(magnitude(3))
            v.tensor_reduce(am_x1, am_x, AX.X, ALU.max).then_inc(amax_part, 1)
            ctx_terms(2)
            largest(gx, 2)
            ctx_terms(3)
            scales(am_x1, rec_x, sc_x, sc_x20, dq_x, 2, x_scale_made)
            ctx_terms(4)
            link(v.tensor_tensor(dequant, dq_x, dq_c, ALU.mult))
            ctx_terms(5)
            quantise_x(0)
            ctx_terms(6)
            quantise_x(1)
            attend(0)
            ctx_terms(7)
            inverse(0)
            quantise_x(2)
            attend(1)
            x_low(0, 0)
            x_low(1, 1)
            inverse(1)
            dve.wait_ge(gate_hi_made, 1)
            v.tensor_tensor(gate_hl[:, :, E:2 * E], gate[:, :].rearrange("p (c e) -> p c e", c=DC),
                            gate_hl[:, :, 0:E].bitcast(F32), ALU.subtract).then_inc(gate_split, 1)
            quantise_x(3)
            x_low(2, 2)
            attend(2)
            x_low(3, 3)
            inverse(2)
            attend(3)
            x_low(4, 4)
            inverse(3)
            x_low(5, 5)
            split_lo(v, LO_GATING[0])
            v.memset(hbuf[:, :, P:2 * P].rearrange("p k (a f) -> p k a f", a=2)[:, :, :, REST:DUP], 0.0)
            x_low(6, 6)
            x_low(7, 7)
            split_lo(v, LO_GATING[1])

            def bc_e(a):
                return a.unsqueeze(2).broadcast_to([P, NT, E])

            def bc_i(a):
                return a.unsqueeze(1).broadcast_to([P, NT, E])

            logits = route_ps[:, 0:NT * 2 * E].rearrange("p (i a e) -> p i a e", a=2, e=E)

            def softmax_shift():
                dve.wait_ge(gate_done, NT)
                link(v.tensor_copy(ta, logits[:, :, 0, :]))
                link(v.tensor_tensor(ta, ta, logits[:, :, 1, :], ALU.add))
                link(v.tensor_reduce(red, ta, AX.X, ALU.max))
                v.tensor_tensor(tb, ta, bc_e(red), ALU.subtract).then_inc(shifted, 1)

            def top_two():
                dve.wait_ge(exp_made, 1)
                link(v.tensor_reduce(red, ta, AX.X, ALU.add))
                link(v.reciprocal(red2[:, :], red))
                link(v.tensor_tensor(probs, ta, bc_e(red2[:, :]), ALU.mult))
                for i in range(NT):
                    last = v.max(top[:, i, :], probs[:, i, :])
                link(last)
                for i in range(NT):
                    last = v.max_index(top_e[:, i, :], top[:, i, :], probs[:, i, :])
                link(last)
                dve.wait_ge(consts_made, 2)
                v.tensor_tensor(e1, bc_i(iota_p[:, 0:E]), bc_e(top_e[:, :, 0]), ALU.is_equal)
                link(v.tensor_tensor(e2, bc_i(iota_p[:, 0:E]), bc_e(top_e[:, :, 1]), ALU.is_equal))
                v.tensor_tensor(chosen[:, 0:NT, :], e1, e2, ALU.add).then_inc(chosen_made, 1)

            ntl, toff, tinc = nt_t[:, 0:E], nt_t[:, E:2 * E], nt_t[:, 2 * E:3 * E]
            rank = route_ps[:, 128:128 + NT * E].rearrange("p (i e) -> p i e", e=E)
            count = route_ps[:, 256:256 + E]

            def first_slots():
                dve.wait_ge(prefix_done, 1)
                more = rt2[:, 0:E * NT].rearrange("p (e m) -> p e m", m=NT)
                link(v.tensor_tensor(more, count.unsqueeze(2).broadcast_to([P, E, NT]),
                                     thr.unsqueeze(1).broadcast_to([P, E, NT]), ALU.is_gt))
                link(v.tensor_reduce(ntl, more, AX.X, ALU.add))
                sq = rt2[:, 0:E * E].rearrange("p (a b) -> p a b", b=E)
                link(v.tensor_tensor(sq, ntl.unsqueeze(1).broadcast_to([P, E, E]), before, ALU.mult))
                link(v.tensor_reduce(toff, sq, AX.X, ALU.add))
                link(v.tensor_tensor(tinc, toff, ntl, ALU.add))
                link(v.tensor_scalar(ntl, toff, float(P), None, ALU.mult))

            def pair_slots():
                link(v.tensor_tensor(slots, rank, bc_i(ntl), ALU.add))
                link(v.tensor_tensor(ta, slots, e1, ALU.mult))
                link(v.tensor_tensor(tb, slots, e2, ALU.mult))
                v.tensor_reduce(posf[:, 0:NT], ta, AX.X, ALU.add)
                link(v.tensor_reduce(posf[:, NT:2 * NT], tb, AX.X, ALU.add))
                link(v.tensor_copy(pos_i, posf))
                v.tensor_scalar(pos_p, pos_i, P - 1, None, ALU.bitwise_and)
                link(v.tensor_scalar(pos_j, pos_i, 7, None, ALU.logical_shift_right))

            def tile_one_hots():
                link(v.tensor_tensor(onehot_t, iota_j.unsqueeze(1).broadcast_to([P, NPAIR, 32]),
                                     pos_j.unsqueeze(2).broadcast_to([P, NPAIR, 32]), ALU.is_equal))
                v.tensor_tensor(onehot_t, onehot_t, tok_id.unsqueeze(2).broadcast_to([P, NPAIR, 32]), ALU.mult)

            def place_one_hots():
                v.tensor_tensor(onehot_p, iota_p.unsqueeze(1).broadcast_to([P, NPAIR, P]),
                                pos_p.unsqueeze(2).broadcast_to([P, NPAIR, P]), ALU.is_equal).then_inc(onehot_made, 1)

            def slot_tables():
                dve.wait_ge(table_done, 1)
                empty, row = rt2[:, 64:96], rt2[:, 96:128]
                v.tensor_scalar(empty, route_ps[:, 320:352], 0.0, 2.0 * TOPK * TOK, ALU.is_equal, ALU.mult)
                link(v.tensor_scalar(row, route_ps[:, 320:352], 1.0, None, ALU.subtract))
                link(v.tensor_copy(dest_of, row))
                link(v.tensor_scalar(token_of, dest_of, TOK - 1, None, ALU.bitwise_and))
                v.tensor_tensor(dest_of, row, empty, ALU.add).then_inc(table_made, 1)

            def tile_experts():
                sq = mx_buf[0:1, 0:32 * E].rearrange("p (j e) -> p j e", e=E)
                link(v.tensor_tensor(sq, tinc[0:1, :].unsqueeze(1).broadcast_to([1, 32, E]),
                                     iota_j[0:1, :].unsqueeze(2).broadcast_to([1, 32, E]), ALU.is_le))
                link(v.tensor_reduce(rt2[0:1, 0:32], sq, AX.X, ALU.add))
                v.tensor_scalar(ex_row[:, :], rt2[0:1, 0:32], float(E - 1), float(NSH), ALU.min, ALU.add) \
                    .then_inc(experts_made, 1)

            def mix(b):
                tiles = (2 * b, 2 * b + 1)
                for k in range(TOPK):
                    dve.wait_ge(y_loaded[k][b], 16)
                    for i in tiles:
                        h = i % 2
                        a = x1[:, i, :]
                        last = v.scalar_tensor_tensor(a, y_buf[:, k, b, h * D:(h + 1) * D],
                                                      top[:, i, k:k + 1], a, ALU.mult, ALU.add)
                        if k == TOPK - 1:
                            last.then_inc(mixed, 1)
                    if k == 0:
                        link(last)

            def step(s, sk):
                if exists(s + 2) and turns(s + 2):
                    x_low(turned(s + 2), turned(sk + 2))
                if exists(s + 1):
                    dve.wait_ge(silu_made, s + 2)
                    if not static(s) or s >= 1:
                        dve.wait_ge(hT_in_psum, s)
                    u_ps = up_ps[(sk + 1) % 2][:, INTER:UP]
                    g, h = sil[:, (sk + 1) % 2, :], hbuf[:, (sk + 1) % 2, :]
                    v.tensor_tensor(h[:, 0:INTER], g, u_ps, ALU.mult)
                    v.tensor_tensor(h[:, P + DUP:P + DUP + REST], g[:, P:INTER], u_ps[:, P:INTER], ALU.mult) \
                        .then_inc(h_made, 1)
                if exists(s):
                    dve.wait_ge(hT_hi_made, s + 1)
                    v.tensor_tensor(hT_lo[:, sk % 2, :], hT_ps[:, 0:D], hT_hi[:, sk % 2, :].bitcast(F32),
                                    ALU.subtract).then_inc(hT_split, 1)
                if exists(s - 1) and not routed(s - 1) and closes(s - 1):
                    n = s - 1
                    dve.wait_ge(y_done, n + 1)
                    a = x1[:, token_tile(n), :]
                    v.tensor_tensor(a, a, y_ps[index(sk - 1) % 2][:, 0:D], ALU.add).then_inc(z_added, 1)

            softmax_shift()
            split_lo(v, LO_GATING[2])
            extra = {-1: [top_two], 1: [first_slots], 2: [pair_slots, tile_one_hots],
                     3: [place_one_hots], 5: [slot_tables], 6: [tile_experts]}

            def with_extras(s, sk):
                for stage in extra.get(s, ()) if static(s) else ():
                    stage()
                step(s, sk)
                n = s - (N0 - 2 - len(LO_STEPS))
                if static(s) and 0 <= n < len(LO_STEPS):
                    split_lo(v, LO_STEPS[n])

            with_extras(-2, -2)
            split_lo(v, LO_GATING[3])
            run_steps(dve, -1, NTILE + 1, with_extras)
            dve.wait_ge(z_added, NT)
            for b in range(B):
                mix(b)

        @block.tensor
        def _(pe):
            mm, tr, PE = nc.tensor.matmul, nc.tensor.transpose, mybir.EngineType.PE

            def amax(n, part):
                pe.wait_ge(amax_part, n)
                mm(att_ps[3 - n][0:1, 0:P], part, ident[:, :], start=True, stop=True).then_inc(amax_row, 1)
                pe.wait_ge(amax_one, n)
                mm(att_ps[3 - n][:, P:P + 1], ones_row[0:1, :], (gc, gx)[n - 1], start=True, stop=True) \
                    .then_inc(amax_all, 1)

            pe.wait_ge(consts_made, 1)
            for i in range(NT):
                if i == 2:
                    amax(1, am_c)
                pe.wait_ge(y_made, i + 1)
                for c in range(DC):
                    last = tr(bank[i // 2][:, c * S + (i % 2) * P:c * S + (i % 2) * P + P],
                              y_norm[:, i * D + c * P:i * D + (c + 1) * P], ident[:, :])
                last.then_inc(yT_done, 1)
            amax(2, am_x1)

            def attention(b):
                pe.wait_ge(x_quant, b + 1)
                pe.wait_ge(ctx_quant, DC * (b + 1))
                for h in range(2):
                    for c in range(DC):
                        last = mm(att_ps[b][:, h * D:(h + 1) * D],
                                  q_xT[:, b % 2, c * S + h * P:c * S + (h + 1) * P], q_ctx[:, DC * b + c, :],
                                  start=(c == 0), stop=(c == DC - 1))
                last.then_inc(att_done, 1)

            def transpose_x(u, src):
                for c in range(DC):
                    last = tr(xT_ps[u % 2][:, c * P:(c + 1) * P], src[:, c * P:(c + 1) * P], ident[:, :])
                last.then_inc(xT_in_psum, 1)

            def transpose_t(i):
                pe.wait_ge(t_made, i + 1)
                transpose_x(i, r1[:, i, :])

            def gate_logits(i):
                pe.wait_ge(xT_split, i + 1)
                if i == 0:
                    pe.wait_ge(gate_split, 1)
                for c in range(DC):
                    o, k = i * 2 * E, slice(c * P, (c + 1) * P)
                    mm(route_ps[:, o:o + 2 * E], xT_hi[:, i % 2, k], gate_hl[:, c, :], start=(c == 0), stop=False)
                    last = mm(route_ps[:, o:o + E], xT_lo[:, i % 2, k], gate_hl[:, c, 0:E],
                              start=False, stop=(c == DC - 1))
                last.then_inc(gate_done, 1)

            attention(0)
            attention(1)
            transpose_t(0)
            transpose_t(1)
            attention(2)
            for i in range(NT):
                gate_logits(i)
                if i + 2 < NT:
                    transpose_t(i + 2)
                if i == 1:
                    attention(3)

            def prefix():
                pe.wait_ge(chosen_made, 1)
                dst = route_ps[:, 128:128 + (NT + 1) * E]
                mm(dst, lower[:, :], chosen[:, :, :].rearrange("p i e -> p (i e)"), start=True, stop=False)
                for j in range(NT):
                    last = mm(route_ps[:, 128 + (j + 1) * E:128 + (NT + 1) * E], ones_bf[:, :],
                              chosen[:, j:j + 1, :].broadcast_to([P, NT - j, E]), start=False, stop=(j == NT - 1))
                last.then_inc(prefix_done, 1)

            def slot_table():
                pe.wait_ge(onehot_made, 1)
                for q in range(NPAIR):
                    last = mm(route_ps[:, 320:352], onehot_p[:, q, :], onehot_t[:, q, :],
                              start=(q == 0), stop=(q == NPAIR - 1))
                last.then_inc(table_done, 1)

            slot_of = {}

            def load_slots(n, count):
                _, got = nc.values_load_multi_w_load_instructions(
                    ex_row[0:1, bass.ds(n - N0, count)], engines=(PE,), min_val=NSH, max_val=NW - 1,
                    skip_runtime_bounds_check_because="the table's values are clamped to the slots")
                return got

            def body_start(s):
                for k, e in enumerate(load_slots(s - 1, UNROLL + 2)):
                    slot_of[LOOP0 - 1 + k] = e

            def weights_of(sk):
                if not routed(sk):
                    return (sk if sk < N0 else sk - N1) % NSH
                return slot_of[sk]

            def step(s, sk):
                if static(s):
                    for n in (s - 1, s, s + 1):
                        if exists(n) and routed(n) and n not in slot_of:
                            slot_of[n] = load_slots(n, 1)[0]
                if exists(s + 2) and turns(s + 2):
                    n = s + 2
                    if routed(n):
                        j, jk = n - N0, sk + 2 - N0
                        pe.wait_ge(x_gathered[jk % XSLOT], 16 * (j // XSLOT + 1) if static(n)
                                   else (s - sk) * (16 // XSLOT) + 16 * (jk // XSLOT + 1))
                        src = xg[jk % XSLOT]
                    else:
                        src = r1[:, token_tile(n), :]
                    transpose_x(turned(sk + 2), src)
                if exists(s + 1):
                    n = s + 1
                    if opens(n):
                        pe.wait_ge(xT_split, turned(n) + 1)
                    if static(n) and n < NSH:
                        pe.wait_ge(w_lo_made, 2 * n + 2)
                    if static(n) and n == N0:
                        pe.wait_ge(w_lo_made, lo_before(2 * NW))
                        pe.wait_ge(w_lo_made_v, len(LO_ON_DVE))
                    e = weights_of(sk + 1)
                    x = turned(sk + 1) % 2
                    q = 0
                    for c in range(DC):
                        for a, wt, row in ((xT_hi, w_hi, WROW), (xT_lo, w_hi, WROW), (xT_hi, w_lo, WMAIN)):
                            last = mm(up_ps[(sk + 1) % 2][:, 0:UP], a[:, x, c * P:(c + 1) * P],
                                      wt[:, bass.ds(e * row + c * UP, UP)], start=(q == 0), stop=(q == 3 * DC - 1))
                            q += 1
                    last.then_inc(up_done, 1)
                if exists(s):
                    pe.wait_ge(h_made, s + 1)
                    if not static(s) or s >= 1:
                        pe.wait_ge(hT_split, s)
                    for c in range(2):
                        last = tr(hT_ps[:, c * P:(c + 1) * P], hbuf[:, sk % 2, c * P:(c + 1) * P], ident[:, :])
                    last.then_inc(hT_in_psum, 1)
                if exists(s - 1):
                    n = s - 1
                    if not exists(s):
                        pe.wait_ge(hT_split, n + 1)
                    if opens(n):
                        emptied_wait(pe, n)
                    e = weights_of(sk - 1)
                    d0, s0 = DC * UP, WMAIN
                    o, b2 = y_ps[index(sk - 1) % 2][:, 0:D], (sk - 1) % 2
                    first, last = opens(n), closes(n)
                    mm(o, hT_hi[:, b2, 0:P], w_hi[:, bass.ds(e * WROW + d0, D)], start=first, stop=False)
                    mm(o, hT_lo[:, b2, 0:P], w_hi[:, bass.ds(e * WROW + d0, D)], start=False, stop=False)
                    mm(o, hT_hi[:, b2, 0:P], w_lo[:, bass.ds(e * WMAIN + d0, D)], start=False, stop=False)
                    mm(o, hT_hi[:, b2, P:2 * P], w_hi[:, bass.ds(e * WROW + s0, D)], start=False, stop=False)
                    mm(o, hT_lo[:, b2, P:2 * P], w_hi[:, bass.ds(e * WROW + s0, D)], start=False, stop=last) \
                        .then_inc(y_done, 1)

            extra = {0: prefix, 4: slot_table, N0 - 2: lambda: pe.wait_ge(experts_made, 1)}

            def with_extras(s, sk):
                step(s, sk)
                if static(s) and s in extra:
                    extra[s]()

            run_steps(pe, -2, NTILE + 1, with_extras, body_start)


def kernel(**inputs):
    import numpy as np
    import concourse.bacc as bacc
    from concourse.bass_utils import run_bass_kernel_spmd

    a = {k: np.ascontiguousarray(v) for k, v in inputs.items()}
    w1, w2, w3 = a["L0_ffn_w1"], a["L0_ffn_w2"], a["L0_ffn_w3"]
    s1, s2, s3 = a["L0_ffn_sw1"], a["L0_ffn_sw2"], a["L0_ffn_sw3"]
    w1 = np.concatenate([s1.reshape(NSH, INTER, D), w1])
    w3 = np.concatenate([s3.reshape(NSH, INTER, D), w3])
    w2 = np.concatenate([s2.reshape(D, NSH, INTER).transpose(1, 0, 2), w2]).transpose(0, 2, 1)
    rows = np.zeros((NW, P, WROW), np.float32)
    for c in range(DC):
        cols = slice(c * P, (c + 1) * P)
        rows[:, :, c * UP:c * UP + INTER] = w1[:, :, cols].transpose(0, 2, 1)
        rows[:, :, c * UP + INTER:(c + 1) * UP] = w3[:, :, cols].transpose(0, 2, 1)
    rows[:, :, DC * UP:WMAIN] = w2[:, 0:P, :]
    rows[:, 0:REST, WMAIN:WROW] = w2[:, P:INTER, :]
    rows[:, DUP:DUP + REST, WMAIN:WROW] = w2[:, P:INTER, :]
    gate = a["L0_ffn_gate_w"].reshape(E, DC, P).transpose(2, 1, 0).reshape(P, DC * E)

    nc = bacc.Bacc("TRN2", target_bir_lowering=False, num_devices=1)
    arrays, args = {}, []
    for name, arr in (("x", a["x"]), ("context", a["ctx_2048"]), ("mask", a["mask_Bx1xS2_ff0"]),
                      ("gate", np.ascontiguousarray(gate)), ("weights", rows)):
        arrays[name + "_dram"] = arr
        args.append(nc.dram_tensor(name + "_dram", arr.shape, mybir.dt.from_np(arr.dtype), kind="ExternalInput").ap())
    out = nc.dram_tensor("out_dram", (B, S, D), mybir.dt.float32, kind="ExternalOutput").ap()
    build(nc, *args, out)
    r = run_bass_kernel_spmd(nc, [arrays], core_ids=[0])
    return r.results[0]["out_dram"]
```
